# Optimizing a Trainium2 kernel written in Bass

```python
import numpy as np
import jax
import jax.numpy as jnp

def _softmax(x, axis=-1):
    return jax.nn.softmax(x, axis=axis)

def _gelu(x):
    return jax.nn.gelu(x, approximate=True)

def _silu(x):
    return jax.nn.silu(x)

def _sigmoid(x):
    return jax.nn.sigmoid(x)

def _layernorm(x, axis=-1, eps=1e-05):
    m = jnp.mean(x, axis=axis, keepdims=True)
    v = jnp.var(x, axis=axis, keepdims=True)
    return (x - m) / jnp.sqrt(v + eps)

def _scatter_add(tgt, idx, src, axis=0):
    return tgt.at[idx].add(src)

def _segment_sum(src, seg, n):
    return jax.ops.segment_sum(src, seg, n)
kernel_name = 'mk_gnn_resnorm_d1_gnn_r32_58c732'

def setup_inputs(seed: int=0):
    np.random.seed(seed)
    _w = jnp.asarray

    def _rec_inputs():
        import jax
        import jax.numpy as jnp
        _gk = jax.random.key(seed)
        x = -0.0002117 + 1 * jax.random.normal(jax.random.fold_in(_gk, 1), (50000, 512), jnp.float32)
        src = jax.random.randint(jax.random.fold_in(_gk, 2), (25000,), 0, 50000, jnp.int32)
        dst = jnp.minimum((50000 * jax.random.uniform(jax.random.fold_in(_gk, 3), (25000,)) ** 2.0).astype(jnp.int32), 49999)
        _o = jnp.argsort(dst, stable=True)
        src = src[_o]
        dst = dst[_o]
        return (x, src, dst)
    x, src, dst = _rec_inputs()

    def _L0_gnn_setup():
        import jax, jax.numpy as jnp
        import numpy as np
        N_NODES = 50000
        D_IN = 512
        D_OUT = 512
        N_EDGES = 25000
        key = jax.random.key(seed)
        kx, ke, k1, k2, k3, k4 = jax.random.split(key, 6)
        x = jax.random.normal(kx, (N_NODES, D_IN), dtype=jnp.float32)
        edge_index = jax.random.randint(ke, (2, N_EDGES), 0, N_NODES, dtype=jnp.int64)
        b1lim = 1.0 / np.sqrt(D_IN)
        b2lim = 1.0 / np.sqrt(D_OUT)
        W1 = jax.random.uniform(k1, (D_IN, D_OUT), jnp.float32, -b1lim, b1lim)
        b1 = jax.random.uniform(k2, (D_OUT,), jnp.float32, -b1lim, b1lim)
        W2 = jax.random.uniform(k3, (D_OUT, D_OUT), jnp.float32, -b2lim, b2lim)
        b2 = jax.random.uniform(k4, (D_OUT,), jnp.float32, -b2lim, b2lim)
        return {'x': x, 'edge_index': edge_index, 'W1': W1, 'b1': b1, 'W2': W2, 'b2': b2}
    _L0_gnn_all = _L0_gnn_setup()
    _L0_gnn_in = {k: v for k, v in _L0_gnn_all.items() if k in ('W1', 'b1', 'W2', 'b2')}
    del _L0_gnn_all
    return {'x': x, 'src': src, 'dst': dst, 'L0_gnn_W1': _L0_gnn_in['W1'], 'L0_gnn_b1': _L0_gnn_in['b1'], 'L0_gnn_W2': _L0_gnn_in['W2'], 'L0_gnn_b2': _L0_gnn_in['b2']}

def reference(x, src, dst, L0_gnn_W1, L0_gnn_b1, L0_gnn_W2, L0_gnn_b2):
    import jax
    import jax.numpy as jnp

    def _L0_gnn_ref(x, edge_index, W1, b1, W2, b2):
        import jax, jax.numpy as jnp
        import numpy as np
        N_NODES = 50000
        D_IN = 512
        D_OUT = 512
        N_EDGES = 25000
        src, dst = (edge_index[0], edge_index[1])
        agg = jax.ops.segment_sum(x[src], dst, num_segments=N_NODES)
        h = x + agg
        h = jax.nn.relu(h @ W1 + b1)
        h = h @ W2 + b2
        return jax.nn.relu(h)
    edge_index = jnp.stack([src, dst])
    x = _layernorm(x + _L0_gnn_ref(x, edge_index, L0_gnn_W1, L0_gnn_b1, L0_gnn_W2, L0_gnn_b2), axis=-1)
    return x

_drawn_inputs = setup_inputs


def setup_inputs(seed=0):
    import zlib

    import numpy as np

    out = dict(_drawn_inputs(seed))
    spreads = {}
    factors = {'L0_gnn_b1': 8.0, 'L0_gnn_b2': 3.109}
    for name, (base, spread) in spreads.items():
        noise = np.random.default_rng([zlib.crc32(name.encode()), seed]).standard_normal(out[name].shape)
        drawn = base * np.exp(spread * noise) if base else spread * noise
        out[name] = jnp.asarray(drawn.astype(out[name].dtype))
    for name, factor in factors.items():
        out[name] = (out[name] * factor).astype(out[name].dtype)
    return out
```

```python
import numpy as np
from contextlib import ExitStack

import concourse.bass as bass
from concourse import mybir

F32 = mybir.dt.float32
F32R = mybir.dt.float32r
I32 = mybir.dt.int32
ALU = mybir.AluOpType
ACT = mybir.ActivationFunctionType
AX = mybir.AxisListType

P = 128
TILES = 4
GRAN = 32
PER_WINDOW = P // GRAN
RING = 4
NO_NODE = 65536.0
FAR = float(1 << 20)
EPS = 1e-5
RSQRT_GUESS = float(0x5F3759DF)
NEWTONS = 3
NORM_STEPS = 4 + 3 * NEWTONS


def plan(n_nodes):
    full, rest = divmod(n_nodes, TILES * P)
    tail_rows = next(r for r in range(P, 0, -16) if rest % r == 0) if rest else 0
    tail_tiles = rest // tail_rows if rest else 0
    return full, tail_rows, tail_tiles


def granule_columns(n_gran_all):
    return n_gran_all // (2 * P)


def gnn_layer(nc, x, edges, W1, b1, W2, b2, tile_low, consts, out):
    N, D = x.shape
    K = D // P
    full, tail_rows, tail_tiles = plan(N)
    n_gran_all = edges.shape[0] // GRAN
    GC = granule_columns(n_gran_all)
    groups = full + (1 if tail_tiles else 0)
    FULL, TAIL = (P, TILES), (tail_rows, tail_tiles)
    half = (GC + 1) // 2
    halves = [(a0, a1) for a0, a1 in ((0, half), (half, GC)) if a1 > a0]
    last_granule = n_gran_all - PER_WINDOW

    ctx = ExitStack()
    with ctx:
        def sb(name, shape, dt=F32):
            return ctx.enter_context(nc.sbuf_tensor(name, shape, dt))

        def ps(name, shape=(P, D)):
            return ctx.enter_context(nc.psum_tensor(name, list(shape), F32))

        def sem(name):
            return ctx.enter_context(nc.semaphore(name))

        const = sb("const", [P, 3 * P + 2 * TILES])
        ident, before, node_no = (const[:, i * P:(i + 1) * P] for i in range(3))
        low_of, high_of = const[:, 3 * P:3 * P + TILES], const[:, 3 * P + TILES:]
        ones = sb("ones", [P, P])
        granules = sb("granules", [P, GC, 2 * GRAN], I32)
        ends = sb("ends", [P, 2, GC])
        spread = sb("spread", [P, 2, GC, P])
        part = sb("part", [P, 2, TILES, 2])
        start_end = sb("start_end", [P, 2, TILES])
        n_gran = sb("n_gran", [P, TILES], I32)
        n_round = sb("n_round", [P, TILES], I32)
        rounds_i = sb("rounds_i", [P, 1], I32)
        rounds_f = sb("rounds_f", [P, 1])
        round_row = sb("round_row", [1, P], I32)
        start_row = sb("start_row", [1, TILES * P], I32)
        w_raw = sb("w_raw", [P, 2, K, D])
        w_hi = sb("w_hi", [P, 2, K, D], F32R)
        w_lo = sb("w_lo", [P, 2, K, D], F32R)
        b1_col = sb("b1_col", [P, K])
        b2_all = sb("b2_all", [P, D])
        rec = sb("rec", [P, TILES, 2], I32)
        rec_low = sb("rec_low", [P, TILES])
        local = sb("local", [P, TILES])
        outside = sb("outside", [P, TILES])
        far = sb("far", [P, TILES])
        row_idx = sb("row_idx", [P, TILES], I32)
        gath = sb("gath", [P, TILES, D])
        gath_hi = sb("gath_hi", [P, TILES, D], F32R)
        gath_lo = sb("gath_lo", [P, TILES, D], F32R)
        onehot = sb("onehot", [P, TILES, P], F32R)
        rows = sb("rows", [P, RING * TILES, D])
        h = sb("h", [P, TILES, D])
        hT_hi = sb("hT_hi", [P, K, TILES * P], F32R)
        hT_lo = sb("hT_lo", [P, K, TILES * P], F32R)
        hid = sb("hid", [P, 2, TILES * P])
        hid_hi = sb("hid_hi", [P, K, TILES * P], F32R)
        hid_lo = sb("hid_lo", [P, K, TILES * P], F32R)
        pre = sb("pre", [P, 2, D])
        stats = sb("stats", [P, TILES, 6])
        mean_var = sb("mean_var", [P, TILES, 2])
        var_eps = sb("var_eps", [P, TILES])
        newton = sb("newton", [P, TILES])
        inv_std = sb("inv_std", [P, TILES])
        shift = sb("shift", [P, TILES])

        ps_g1 = [ps(f"ps_g1_{i}") for i in range(2)]
        ps_g2 = [ps(f"ps_g2_{i}") for i in range(2)]
        ps_agg = [ps(f"ps_agg_{i}") for i in range(2)]
        ps_T = [ps(f"ps_T_{i}") for i in range(2)]
        ps_ends = [[ps_g1, ps_g2][c][i] for c in range(2) for i in range(2)]

        const_loaded = sem("const_loaded")
        granules_loaded = sem("granules_loaded")
        w_loaded = sem("w_loaded")
        b_loaded = sem("b_loaded")
        zeroed = sem("zeroed")
        spread_ready = sem("spread_ready")
        ends_ready = sem("ends_ready")
        counted = sem("counted")
        rowed = sem("rowed")
        table_ready = sem("table_ready")
        w_hi_ready = sem("w_hi_ready")
        w_ready = sem("w_ready")
        setup_step = sem("setup_step")
        passed = sem("passed")
        rec_loaded = sem("rec_loaded")
        idx_step = sem("idx_step")
        idx_ready = sem("idx_ready")
        gathered = [sem(f"gathered_{j}") for j in range(TILES)]
        gath_hi_ready = sem("gath_hi_ready")
        gath_lo_ready = sem("gath_lo_ready")
        onehot_ready = sem("onehot_ready")
        agg_done = sem("agg_done")
        h_added = sem("h_added")
        x_loaded = sem("x_loaded")
        T_done = sem("T_done")
        hT_hi_ready = sem("hT_hi_ready")
        hT_lo_ready = sem("hT_lo_ready")
        g1_done = sem("g1_done")
        hid_hi_ready = sem("hid_hi_ready")
        hid_lo_ready = sem("hid_lo_ready")
        g2_done = sem("g2_done")
        g2_read = sem("g2_read")
        res_step = sem("res_step")
        norm_step = sem("norm_step")
        norm_ready = sem("norm_ready")
        normed = sem("normed")
        stored = sem("stored")

        def slot(g, j):
            return bass.ds((g % RING) * TILES + j, 1)

        def rows_before(eng, g):
            return eng.value_load(round_row[0:1, bass.ds(g, 1)], min_val=0, max_val=1 << 20)

        def for_groups(eng, body):
            body(0, FULL, FULL, first=True)
            body(1, FULL, FULL)
            if full > 3:
                with eng.Fori(2, full - 1) as g:
                    body(g, FULL, FULL)
            body(full - 1, FULL, TAIL if tail_tiles else None)
            if tail_tiles:
                body(full, TAIL, None)

        def wait_alone(eng, semaphore, value):
            eng.wait_ge(semaphore, value)
            eng.sem_inc(passed, 1)

        block = ctx.enter_context(nc.Block())

        @block.sync
        def _(sp):
            sp.dma_start(const[:, :], consts).then_inc(const_loaded, 16)
            sp.dma_start(granules[:, :, :], edges[0:GC * P * GRAN, :].rearrange("(a p r) c -> p a (r c)", p=P, r=GRAN)
                         ).then_inc(granules_loaded, 16)
            sp.dma_start(w_raw[:, 0], W1.rearrange("(k p) n -> p k n", p=P)).then_inc(w_loaded, 16)
            sp.dma_start(w_raw[:, 1], W2.rearrange("(k p) n -> p k n", p=P)).then_inc(w_loaded, 16)
            with nc.allow_non_contiguous_dma(reason="a bias of 512 values, once"):
                sp.dma_start(b1_col[:, :], b1.rearrange("(k p) -> p k", p=P)).then_inc(b_loaded, 16)
            sp.dma_start(b2_all[:, :], b2.partition_broadcast(P)).then_inc(b_loaded, 16)

            def load_group(g, shape, slot_used):
                r, n = shape
                if slot_used:
                    sp.wait_ge(x_loaded, 16 * g)
                    sp.wait_ge(stored, 16 * (g - RING + 1))
                elif g:
                    sp.wait_ge(x_loaded, 16 * g)
                sp.dma_start(rows[0:r, bass.ds((g % RING) * TILES, n), :],
                             x[bass.ds(g * TILES * P, r * n), :].rearrange("(j p) d -> p j d", p=r)
                             ).then_inc(x_loaded, 16)
                if not slot_used and g == 0:
                    sp.wait_ge(table_ready, 2)
                first = [sp.value_load(start_row[0:1, bass.ds(g + P * j, 1)], min_val=0,
                                       max_val=last_granule) for j in range(TILES)]
                r0, r1 = rows_before(sp, g), rows_before(sp, g + 1)

                def load_round(rho):
                    sp.wait_ge(idx_ready, rho)
                    load_record(g, [f + (rho - r0) * PER_WINDOW for f in first])

                if isinstance(g, int) and g == 0:
                    r0 = 0
                    load_round(0)
                    with sp.If(r1 > 1):
                        with sp.Fori(1, r1) as rho:
                            load_round(rho)
                else:
                    with sp.Fori(r0, r1) as rho:
                        load_round(rho)

            def load_record(g, starts):
                for j, s in enumerate(starts):
                    at = (s if isinstance(s, int) else s.with_bounds(min_val=0, max_val=last_granule)) * GRAN
                    sp.dma_start(rec[:, j, :], edges[bass.ds(at, P), :]).then_inc(rec_loaded, 16)
                sp.dma_start(rec_low[:, :], tile_low[bass.ds(g, 1), :].partition_broadcast(P)
                             ).then_inc(rec_loaded, 16)

            for g in range(min(RING, full)):
                load_group(g, FULL, False)
            if full > RING:
                with sp.Fori(RING, full) as g:
                    load_group(g, FULL, True)
            if tail_tiles:
                load_group(full, TAIL, full >= RING)
            sp.wait_ge(idx_ready, rows_before(sp, groups))
            load_record(0, [0] * TILES)

        @block.gpsimd
        def _(pool):
            nc.gpsimd.memset(ones[:, :], 1.0).then_inc(zeroed, 1)
            nc.gpsimd.memset(gath[:, :, :], 0.0).then_inc(zeroed, 1)
            pool.wait_ge(zeroed, 2)
            pool.wait_ge(table_ready, 2)
            total = rows_before(pool, groups)
            last_row = pool.to_reg(N - 1)

            def split_gathered(rho, first=False):
                for j in range(TILES):
                    pool.wait_ge(gath_hi_ready, rho * TILES + j + 1)
                    if not first:
                        pool.wait_ge(agg_done, (rho - 1) * TILES + j + 1)
                    nc.gpsimd.tensor_tensor(gath_lo[:, j, :], gath[:, j, :], gath_hi[:, j, :].bitcast(F32),
                                            ALU.subtract).then_inc(gath_lo_ready, 1)

            def gather(rho):
                pool.wait_ge(idx_ready, rho + 1)
                wait_alone(pool, gath_lo_ready, rho * TILES)
                for j in range(TILES):
                    nc.gpsimd.indirect_dma_start(
                        out=gath[:, j, :], out_offset=None, in_=x,
                        in_offset=bass.IndirectOffsetOnAxis(ap=row_idx[:, j:j + 1], axis=0),
                        bounds_check=last_row, oob_is_err=False).then_inc(gathered[j], 16)

            gather(0)
            split_gathered(0, first=True)
            with pool.If(total > 1):
                with pool.Fori(1, total) as rho:
                    gather(rho)
                    split_gathered(rho)

        @block.scalar
        def _(act):
            act.wait_ge(w_loaded, 32)
            nc.scalar.copy(w_hi[:, 0], w_raw[:, 0]).then_inc(w_hi_ready, 1)
            nc.scalar.copy(w_hi[:, 1], w_raw[:, 1]).then_inc(w_hi_ready, 1)
            act.wait_ge(b_loaded, 32)
            act.wait_ge(table_ready, 2)

            def split_gathered(rho):
                act.wait_ge(agg_done, rho * TILES)
                for j in range(TILES):
                    act.wait_ge(gathered[j], (rho + 1) * 16)
                    nc.scalar.copy(gath_hi[:, j, :], gath[:, j, :]).then_inc(gath_hi_ready, 1)

            def more_rounds(r0, r1):
                with act.If(r1 > r0 + 1):
                    with act.Fori(r0 + 1, r1) as rho:
                        split_gathered(rho)

            def split_hT(g, shape, k):
                c = shape[0] * shape[1]
                act.wait_ge(T_done, g * K + k + 1)
                nc.scalar.copy(hT_hi[:, k, 0:c], ps_T[k % 2][:, 0:c]).then_inc(hT_hi_ready, 1)

            def hidden(g, shape, m):
                c = shape[0] * shape[1]
                act.wait_ge(g1_done, g * K + m + 1)
                act.wait_ge(hid_lo_ready, g * K + (m - 1 if m > 1 else 0))
                nc.scalar.activation(hid[:, m % 2, 0:c], ps_g1[m % 2][:, 0:c], ACT.Relu,
                                     bias=b1_col[:, m:m + 1])
                if m == 0:
                    act.wait_ge(g2_done, g * TILES)
                nc.scalar.activation(hid_hi[:, m, 0:c], ps_g1[m % 2][:, 0:c], ACT.Relu,
                                     bias=b1_col[:, m:m + 1]).then_inc(hid_hi_ready, 1)

            def normalise(g, shape):
                r, n = shape
                act.wait_ge(norm_ready, g + 1)
                for j in range(n):
                    y = rows[0:r, slot(g, j), :]
                    nc.scalar.activation(y, y, ACT.Identity, bias=shift[0:r, j:j + 1],
                                         scale=inv_std[0:r, j:j + 1]).then_inc(normed, 1)

            def store(g, shape):
                r, n = shape
                act.wait_ge(normed, g * TILES + n)
                act.wait_ge(stored, g * 16)
                act.dma_start(out[bass.ds(g * TILES * P, r * n), :].rearrange("(j p) d -> p j d", p=r),
                              rows[0:r, bass.ds((g % RING) * TILES, n), :]).then_inc(stored, 16)

            def body(g, shape, then, first=False):
                hidden(g, shape, 0)
                if then:
                    r0, r1 = rows_before(act, g + 1), rows_before(act, g + 2)
                    split_gathered(r0)
                hidden(g, shape, 1)
                hidden(g, shape, 2)
                hidden(g, shape, 3)
                if not first:
                    normalise(g - 1, FULL)
                    store(g - 1, FULL)
                if then:
                    more_rounds(r0, r1)
                    act.wait_ge(g1_done, g * K + K)
                    for k in range(K):
                        split_hT(g + 1, then, k)

            split_gathered(0)
            more_rounds(0, rows_before(act, 1))
            for k in range(K):
                split_hT(0, FULL, k)
            for_groups(act, body)
            g, shape = (full, TAIL) if tail_tiles else (full - 1, FULL)
            normalise(g, shape)
            store(g, shape)
            act.wait_ge(stored, 16 * groups)

        @block.vector
        def _(dve):
            steps = [0]

            def step(ins):
                steps[0] += 1
                ins.then_inc(setup_step, 1)
                dve.wait_ge(setup_step, steps[0])

            step(nc.vector.memset(part[:, :, :, :], 0.0))
            dve.wait_ge(const_loaded, 16)
            dve.wait_ge(granules_loaded, 16)
            nc.vector.tensor_copy(ends[:, 0, :], granules[:, :, 1])
            step(nc.vector.tensor_copy(ends[:, 1, :], granules[:, :, 2 * GRAN - 1]))
            for e in range(2):
                for a in range(GC):
                    last = nc.vector.tensor_scalar(spread[:, e, a, :], ident, ends[:, e, a:a + 1], None, ALU.mult)
            last.then_inc(spread_ready, 1)
            dve.wait_ge(ends_ready, 1)
            for t in range(TILES):
                for e, bound in enumerate((high_of, low_of)):
                    for c, (a0, a1) in enumerate(halves):
                        last = nc.vector.tensor_scalar(
                            spread[:, e, a0:a1, :].rearrange("p a n -> p (a n)"),
                            ps_ends[2 * e + c][:, 0:(a1 - a0) * P], bound[:, t:t + 1], 0.0,
                            ALU.is_lt, ALU.add, accum_out=part[:, 1 - e, t, c:c + 1])
                step(last)
            step(nc.vector.tensor_tensor(start_end[:, :, :], part[:, :, :, 0], part[:, :, :, 1], ALU.add))
            step(nc.vector.scalar_tensor_tensor(n_gran[:, :], start_end[:, 1, :], float(PER_WINDOW - 1),
                                                start_end[:, 0, :], ALU.add, ALU.subtract))
            step(nc.vector.tensor_scalar(n_round[:, :], n_gran[:, :], PER_WINDOW.bit_length() - 1, None,
                                         ALU.arith_shift_right))
            step(nc.vector.tensor_reduce(rounds_i[:, :], n_round[:, :], AX.X, ALU.max))
            nc.vector.tensor_scalar(rounds_f[:, :], rounds_i[:, :], 1.0, None, ALU.max).then_inc(counted, 1)
            dve.wait_ge(rowed, 1)
            nc.vector.tensor_copy(round_row[0:1, :], ps_agg[0][0:1, 0:P]).then_inc(table_ready, 1)
            nc.vector.tensor_copy(start_row[0:1, :], ps_agg[1][0:1, 0:TILES * P]).then_inc(table_ready, 1)

            def indices(rho):
                dve.wait_ge(rec_loaded, (rho + 1) * (16 * (TILES + 1)))
                nc.vector.tensor_tensor(local[:, :], rec[:, :, 1], rec_low[:, :],
                                        ALU.subtract).then_inc(idx_step, 1)
                dve.wait_ge(idx_step, rho * 3 + 1)
                nc.vector.scalar_tensor_tensor(outside[:, :], local[:, :], float(P - 1), local[:, :],
                                               ALU.subtract, ALU.mult).then_inc(idx_step, 1)
                dve.wait_ge(idx_step, rho * 3 + 2)
                nc.vector.tensor_scalar(far[:, :], outside[:, :], 0.0, FAR, ALU.is_gt,
                                        ALU.mult).then_inc(idx_step, 1)
                dve.wait_ge(idx_step, rho * 3 + 3)
                nc.vector.tensor_tensor(row_idx[:, :], far[:, :], rec[:, :, 0],
                                        ALU.add).then_inc(idx_ready, 1)

            def onehots(rho):
                dve.wait_ge(agg_done, rho * TILES)
                for j in range(TILES):
                    last = nc.vector.tensor_scalar(onehot[:, j, :], node_no, local[:, j:j + 1], None,
                                                   ALU.is_equal)
                last.then_inc(onehot_ready, 1)
                for j in range(TILES):
                    dve.wait_ge(gathered[j], (rho + 1) * 16)
                dve.wait_ge(onehot_ready, rho + 1)
                dve.wait_ge(idx_ready, rho + 1)
                indices(rho + 1)

            def add_first(g, shape, rho, j):
                r, n = shape
                dve.wait_ge(agg_done, rho * TILES + j + 1)
                if j < n:
                    nc.vector.tensor_tensor(h[0:r, j, :], ps_agg[j % 2][0:r, :],
                                            rows[0:r, slot(g, j), :], ALU.add).then_inc(h_added, 1)
                else:
                    dve.sem_inc(h_added, 1)

            def add_more(shape, rho, j):
                r, n = shape
                dve.wait_ge(agg_done, rho * TILES + j + 1)
                dve.wait_ge(h_added, rho * TILES + j)
                if j < n:
                    nc.vector.tensor_tensor(h[0:r, j, :], ps_agg[j % 2][0:r, :], h[0:r, j, :],
                                            ALU.add).then_inc(h_added, 1)
                else:
                    dve.sem_inc(h_added, 1)

            def may_add(g):
                dve.wait_ge(x_loaded, (g + 1) * 16)
                dve.wait_ge(T_done, g * K)

            def more_rounds(shape, r0, r1):
                with dve.If(r1 > r0 + 1):
                    with dve.Fori(r0 + 1, r1) as rho:
                        onehots(rho)
                        for j in range(TILES):
                            add_more(shape, rho, j)

            def split_hT(g, shape, k):
                c = shape[0] * shape[1]
                dve.wait_ge(hT_hi_ready, g * K + k + 1)
                nc.vector.tensor_tensor(hT_lo[:, k, 0:c], ps_T[k % 2][:, 0:c],
                                        hT_hi[:, k, 0:c].bitcast(F32), ALU.subtract).then_inc(hT_lo_ready, 1)

            def hidden(g, shape, m):
                c = shape[0] * shape[1]
                dve.wait_ge(hid_hi_ready, g * K + m + 1)
                nc.vector.tensor_tensor(hid_lo[:, m, 0:c], hid[:, m % 2, 0:c],
                                        hid_hi[:, m, 0:c].bitcast(F32), ALU.subtract).then_inc(hid_lo_ready, 1)

            def add_bias(g, shape, t):
                r, n = shape
                if t < n:
                    dve.wait_ge(g2_done, g * TILES + t + 1)
                    nc.vector.tensor_tensor(pre[0:r, t % 2, :], ps_g2[t % 2][0:r, :], b2_all[0:r, :],
                                            ALU.add).then_inc(g2_read, 1)

            def residual(g, shape, t):
                r, n = shape
                if t < n:
                    dve.wait_ge(g2_read, g * TILES + t + 1)
                    y = rows[0:r, slot(g, t), :]
                    nc.vector.scalar_tensor_tensor(y, pre[0:r, t % 2:t % 2 + 1, :], 0.0, y, ALU.max,
                                                   ALU.add).then_inc(res_step, 1)

            def statistics(g, shape, t):
                r, n = shape
                if t < n:
                    wait_alone(dve, res_step, (g * TILES + t) * 2 + 1)
                    nc.vector.bn_stats(stats[0:r, t, :], rows[0:r, slot(g, t), :]).then_inc(res_step, 1)

            def mean_and_variance(g, shape, t):
                r, n = shape
                if t < n:
                    if t == 0:
                        dve.wait_ge(norm_ready, g)
                    wait_alone(dve, res_step, (g * TILES + t) * 2 + 2)
                    last = nc.vector.bn_aggr(mean_var[0:r, t, :], stats[0:r, t, :])
                    if t == n - 1:
                        last.then_inc(norm_step, 1)
                        dve.wait_ge(norm_step, g * NORM_STEPS + 1)
                        nc.vector.tensor_scalar(var_eps[0:r, 0:n], mean_var[0:r, 0:n, 1], EPS, None,
                                                ALU.add).then_inc(norm_step, 1)

            def norm_factors(g, shape):
                r, n = shape

                def link(i, ins):
                    ins.then_inc(norm_step, 1)
                    dve.wait_ge(norm_step, g * NORM_STEPS + i)

                y, t, v = inv_std[0:r, 0:n], newton[0:r, 0:n], var_eps[0:r, 0:n]
                dve.wait_ge(norm_step, g * NORM_STEPS + 2)
                dve.wait_ge(normed, g * TILES)
                link(3, nc.vector.tensor_scalar(newton[0:r, 0:n].bitcast(I32), v.bitcast(I32), 1, None,
                                                ALU.arith_shift_right))
                link(4, nc.vector.tensor_scalar(y.bitcast(I32), t.bitcast(I32), -1.0, RSQRT_GUESS,
                                                ALU.mult, ALU.add))
                for i in range(NEWTONS):
                    link(5 + 3 * i, nc.vector.tensor_tensor(t, y, y, ALU.mult))
                    link(6 + 3 * i, nc.vector.scalar_tensor_tensor(t, t, -0.5, v, ALU.mult, ALU.mult))
                    link(7 + 3 * i, nc.vector.scalar_tensor_tensor(y, t, 1.5, y, ALU.add, ALU.mult))
                nc.vector.scalar_tensor_tensor(shift[0:r, 0:n], mean_var[0:r, 0:n, 0], -1.0,
                                               y, ALU.mult, ALU.mult).then_inc(norm_ready, 1)

            def body(g, shape, then, first=False):
                if then:
                    r0, r1 = rows_before(dve, g + 1), rows_before(dve, g + 2)
                if not first:
                    norm_factors(g - 1, FULL)
                hidden(g, shape, 0)
                if then:
                    onehots(r0)
                hidden(g, shape, 1)
                hidden(g, shape, 2)
                hidden(g, shape, 3)
                if then:
                    may_add(g + 1)
                    add_first(g + 1, then, r0, 0)
                    add_first(g + 1, then, r0, 1)
                add_bias(g, shape, 0)
                if then:
                    add_first(g + 1, then, r0, 2)
                residual(g, shape, 0)
                if then:
                    add_first(g + 1, then, r0, 3)
                statistics(g, shape, 0)
                if then:
                    more_rounds(then, r0, r1)
                add_bias(g, shape, 1)
                mean_and_variance(g, shape, 0)
                residual(g, shape, 1)
                if then:
                    split_hT(g + 1, then, 0)
                statistics(g, shape, 1)
                if then:
                    split_hT(g + 1, then, 1)
                add_bias(g, shape, 2)
                mean_and_variance(g, shape, 1)
                residual(g, shape, 2)
                if then:
                    split_hT(g + 1, then, 2)
                statistics(g, shape, 2)
                if then:
                    split_hT(g + 1, then, 3)
                add_bias(g, shape, 3)
                mean_and_variance(g, shape, 2)
                residual(g, shape, 3)
                statistics(g, shape, 3)
                mean_and_variance(g, shape, 3)

            dve.wait_ge(table_ready, 2)
            dve.wait_ge(zeroed, 2)
            indices(0)
            dve.wait_ge(w_hi_ready, 2)
            for i in range(2):
                last = nc.vector.tensor_tensor(w_lo[:, i], w_raw[:, i], w_hi[:, i].bitcast(F32), ALU.subtract)
            last.then_inc(w_ready, 1)
            onehots(0)
            may_add(0)
            for j in range(TILES):
                add_first(0, FULL, 0, j)
            more_rounds(FULL, 0, rows_before(dve, 1))
            for k in range(K):
                split_hT(0, FULL, k)
            dve.wait_ge(b_loaded, 32)
            for_groups(dve, body)
            norm_factors(*((full, TAIL) if tail_tiles else (full - 1, FULL)))

        @block.tensor
        def _(pe):
            pe.wait_ge(zeroed, 2)
            pe.wait_ge(spread_ready, 1)
            for e in range(2):
                for c, (a0, a1) in enumerate(halves):
                    last = nc.tensor.matmul(ps_ends[2 * e + c][:, 0:(a1 - a0) * P], ones[:, :],
                                            spread[:, e, a0:a1, :].rearrange("p a n -> p (a n)"),
                                            start=True, stop=True)
            last.then_inc(ends_ready, 1)
            pe.wait_ge(counted, 1)
            nc.tensor.matmul(ps_agg[0][0:1, 0:P], rounds_f[:, :], before, start=True, stop=True)
            for j in range(TILES):
                last = nc.tensor.matmul(ps_agg[1][0:1, j * P:(j + 1) * P], start_end[:, 0, j:j + 1], ident,
                                        start=True, stop=True)
            last.then_inc(rowed, 1)
            pe.wait_ge(table_ready, 2)
            pe.wait_ge(w_ready, 1)

            def product(out_, a_hi, a_lo, b_hi, b_lo, start, stop):
                nc.tensor.matmul(out_, a_hi, b_hi, start=start, stop=False)
                nc.tensor.matmul(out_, a_hi, b_lo, start=False, stop=False)
                return nc.tensor.matmul(out_, a_lo, b_hi, start=False, stop=stop)

            def aggregate(rho, shape, tiles=range(TILES)):
                r = shape[0]
                pe.wait_ge(onehot_ready, rho + 1)
                for j in tiles:
                    pe.wait_ge(gath_lo_ready, rho * TILES + j + 1)
                    pe.wait_ge(h_added, rho * TILES + (j - 1 if j > 1 else 0))
                    nc.tensor.matmul(ps_agg[j % 2][0:r, :], onehot[:, j, 0:r], gath_hi[:, j, :],
                                     start=True, stop=False)
                    nc.tensor.matmul(ps_agg[j % 2][0:r, :], onehot[:, j, 0:r], gath_lo[:, j, :],
                                     start=False, stop=True).then_inc(agg_done, 1)

            def more_rounds(shape, r0, r1):
                with pe.If(r1 > r0 + 1):
                    with pe.Fori(r0 + 1, r1) as rho:
                        aggregate(rho, shape)

            def transposes(g, shape, k):
                r, n = shape
                pe.wait_ge(hT_lo_ready, g * K + (k - 1 if k > 1 else 0))
                for j in range(n):
                    last = nc.tensor.transpose(ps_T[k % 2][:, j * r:(j + 1) * r],
                                               h[0:r, j, k * P:(k + 1) * P], ident[0:r, 0:r])
                last.then_inc(T_done, 1)

            def first_product(g, shape, m):
                c = shape[0] * shape[1]
                pe.wait_ge(hid_hi_ready, g * K + (m - 1 if m > 1 else 0))
                for k in range(K):
                    if m == 0:
                        pe.wait_ge(hT_lo_ready, g * K + k + 1)
                    last = product(ps_g1[m % 2][:, 0:c],
                                   w_hi[:, 0, k, m * P:(m + 1) * P], w_lo[:, 0, k, m * P:(m + 1) * P],
                                   hT_hi[:, k, 0:c], hT_lo[:, k, 0:c], k == 0, k == K - 1)
                last.then_inc(g1_done, 1)

            def second_product(g, shape, t):
                r, n = shape
                if t >= n:
                    return
                pe.wait_ge(g2_read, g * TILES + (t - 1 if t > 1 else 0))
                for k in range(K):
                    if t == 0:
                        pe.wait_ge(hid_lo_ready, g * K + k + 1)
                    last = product(ps_g2[t % 2][0:r, :],
                                   hid_hi[:, k, t * r:(t + 1) * r], hid_lo[:, k, t * r:(t + 1) * r],
                                   w_hi[:, 1, k, :], w_lo[:, 1, k, :], k == 0, k == K - 1)
                last.then_inc(g2_done, 1)

            def body(g, shape, then, first=False):
                for m in range(K):
                    first_product(g, shape, m)
                if then:
                    r0, r1 = rows_before(pe, g + 1), rows_before(pe, g + 2)
                    aggregate(r0, then, (0, 1))
                second_product(g, shape, 0)
                if then:
                    aggregate(r0, then, (2, 3))
                    more_rounds(then, r0, r1)
                second_product(g, shape, 1)
                if then:
                    pe.wait_ge(h_added, r1 * TILES)
                    transposes(g + 1, then, 0)
                    transposes(g + 1, then, 1)
                second_product(g, shape, 2)
                if then:
                    transposes(g + 1, then, 2)
                    transposes(g + 1, then, 3)
                second_product(g, shape, 3)

            aggregate(0, FULL)
            r1 = rows_before(pe, 1)
            more_rounds(FULL, 0, r1)
            pe.wait_ge(h_added, r1 * TILES)
            for k in range(K):
                transposes(0, FULL, k)
            for_groups(pe, body)


def kernel(x, src, dst, L0_gnn_W1, L0_gnn_b1, L0_gnn_W2, L0_gnn_b2):
    import concourse.bacc as bacc
    from concourse.bass_utils import run_bass_kernel_spmd

    x = np.ascontiguousarray(x)
    n_nodes, n_edges = x.shape[0], src.shape[0]
    full, tail_rows, tail_tiles = plan(n_nodes)
    GC = -(-(-(-n_edges // GRAN) + PER_WINDOW) // P)
    edges = np.full((2 * GC * P * GRAN, 2), int(NO_NODE), np.int32)
    edges[:n_edges, 0], edges[:n_edges, 1] = src, dst
    low = np.full((P, TILES), float(n_nodes), np.float32)
    high = low.copy()
    for g in range(full):
        low[g] = (g * TILES + np.arange(TILES)) * P
        high[g] = low[g] + P
    for j in range(tail_tiles):
        low[full, j] = full * TILES * P + j * tail_rows
        high[full, j] = low[full, j] + tail_rows
    i = np.arange(P)
    consts = np.concatenate([np.eye(P), i[:, None] < i[None, :], np.tile(i, (P, 1)), low, high],
                            axis=1).astype(np.float32)
    arrays = {"x": x, "edges": edges, "W1": L0_gnn_W1, "b1": L0_gnn_b1, "W2": L0_gnn_W2, "b2": L0_gnn_b2,
              "tile_low": low, "consts": consts}
    arrays = {k: np.ascontiguousarray(v) for k, v in arrays.items()}
    nc = bacc.Bacc("TRN2", target_bir_lowering=False, num_devices=1)
    args = [nc.dram_tensor(f"in_{k}", a.shape, mybir.dt.from_np(a.dtype), kind="ExternalInput").ap()
            for k, a in arrays.items()]
    out = nc.dram_tensor("out_0", x.shape, F32, kind="ExternalOutput").ap()
    gnn_layer(nc, *args, out)
    r = run_bass_kernel_spmd(nc, [{f"in_{k}": a for k, a in arrays.items()}], core_ids=[0])
    return r.results[0]["out_0"]
```

```python
import numpy as np
from contextlib import ExitStack

import concourse.bass as bass
from concourse import mybir

F32 = mybir.dt.float32
F32R = mybir.dt.float32r
I32 = mybir.dt.int32
ALU = mybir.AluOpType
ACT = mybir.ActivationFunctionType
AX = mybir.AxisListType

P = 128
TILES = 4
FRONT, BACK = (0, 1), (2, 3)
GRAN = 32
PER_WINDOW = P // GRAN
RING = 4
NO_NODE = 65536.0
FAR = float(1 << 20)
EPS = 1e-5
RSQRT_GUESS = float(0x5F3759DF)
NEWTONS = 3
NORM_STEPS = 4 + 3 * NEWTONS
W_GROUP = 2
PIECE = 2048


def plan(n_nodes):
    full, rest = divmod(n_nodes, TILES * P)
    tail_rows = next(r for r in range(P, 0, -16) if rest % r == 0) if rest else 0
    tail_tiles = rest // tail_rows if rest else 0
    return full, tail_rows, tail_tiles


def granule_columns(n_gran_all):
    return n_gran_all // (2 * P)


class Windows:
    def __init__(self, name, ahead, width, sb, sem, gath_hi, gath_lo):
        self.ahead = ahead
        self.rec = sb(name + "_rec", [P, TILES, 2], I32)
        self.rec_low = sb(name + "_rec_low", [P, TILES])
        self.local = sb(name + "_local", [P, TILES])
        self.outside = sb(name + "_outside", [P, TILES])
        self.far = sb(name + "_far", [P, TILES])
        self.row_idx = sb(name + "_row_idx", [P, TILES], I32)
        self.gath = sb(name + "_gath", [P, TILES, width])
        self.gath_hi, self.gath_lo = gath_hi, gath_lo
        self.onehot = sb(name + "_onehot", [P, TILES, P], F32R)
        self.rec_loaded = sem(name + "_rec_loaded")
        self.idx_step = sem(name + "_idx_step")
        self.idx_ready = sem(name + "_idx_ready")
        self.gathered = [sem(f"{name}_gathered_{j}") for j in range(TILES)]
        self.hi_ready = sem(name + "_hi_ready")
        self.lo_ready = sem(name + "_lo_ready")
        self.onehot_ready = sem(name + "_onehot_ready")
        self.agg_done = sem(name + "_agg_done")
        self.added = sem(name + "_added")

    def round_before(self, n, j):
        return (n if self.ahead else n - 1) * TILES + j + 1


def gnn_layer(nc, x, edges, W1, b1, W2, b2, tile_low, consts, edge_no, in_piece, out):
    N, D = x.shape
    K = D // P
    full, tail_rows, tail_tiles = plan(N)
    n_gran_all = edges.shape[0] // GRAN
    GC = granule_columns(n_gran_all)
    groups = full + (1 if tail_tiles else 0)
    FULL, TAIL = (P, TILES), (tail_rows, tail_tiles)
    last_granule = n_gran_all - PER_WINDOW
    n_sort = GC * P * GRAN
    by_dst = nc.dram_tensor("by_dst", edges.shape, I32, kind="Internal").ap()

    ctx = ExitStack()
    with ctx:
        def sb(name, shape, dt=F32):
            return ctx.enter_context(nc.sbuf_tensor(name, shape, dt))

        def ps(name, shape=(P, D)):
            return ctx.enter_context(nc.psum_tensor(name, list(shape), F32))

        def sem(name):
            return ctx.enter_context(nc.semaphore(name))

        const = sb("const", [P, (3 + 2 * TILES) * P])
        ident, before, node_no = (const[:, i * P:(i + 1) * P] for i in range(3))
        low_row = const[:, 3 * P:(3 + TILES) * P]
        high_row = const[:, (3 + TILES) * P:]
        ones = sb("ones", [P, P])
        granules = sb("granules", [P, GC, 2 * GRAN], I32)
        following = sb("following", [P, GC, 2 * GRAN], I32)
        falls = sb("falls", [P, GC, GRAN])
        n_falls = sb("n_falls", [P, 1])
        unsorted = sb("unsorted", [1, 1], I32)
        rank = sb("rank", [P, GC * GRAN])
        rank_part = sb("rank_part", [P, GC * GRAN])
        rank_i = sb("rank_i", [P, GC * GRAN], I32)
        number = sb("number", [P, GC * GRAN])
        pair = sb("pair", [P, 2], I32)
        pair_rank = sb("pair_rank", [P, 1], I32)
        ends = sb("ends", [P, 2, GC])
        ones_r = sb("ones_r", [P, P], F32R)
        n_gran = sb("n_gran", [1, TILES * P], I32)
        n_round = sb("n_round", [1, TILES * P], I32)
        most_rounds = sb("most_rounds", [1, P], I32)
        n_extra = sb("n_extra", [1, P])
        n_extra_col = sb("n_extra_col", [P, 1])
        extra_row = sb("extra_row", [1, P], I32)
        start_row = sb("start_row", [1, TILES * P], I32)
        w_hi = sb("w_hi", [P, 2, K, D], F32R)
        w_lo = sb("w_lo", [P, 2, K, D], F32R)
        b1_col = sb("b1_col", [P, K])
        b2_all = sb("b2_all", [P, D])
        first = Windows("first", 0, D, sb, sem, sb("gath_hi", [P, TILES, D], F32R),
                        sb("gath_lo", [P, TILES, D], F32R))
        extra = Windows("extra", 1, D, sb, sem, sb("extra_gath_hi", [P, TILES, D], F32R),
                        sb("extra_gath_lo", [P, TILES, D], F32R))
        rows = sb("rows", [P, RING * TILES, D])
        w_raw = rows[:, W_GROUP * TILES:W_GROUP * TILES + 2 * K, :].rearrange("p (i k) n -> p i k n", i=2)
        h = sb("h", [P, TILES, D])
        hT_hi = sb("hT_hi", [P, K, TILES * P], F32R)
        hT_lo = sb("hT_lo", [P, K, TILES * P], F32R)
        hid = sb("hid", [P, 2, TILES * P])
        hid_hi = sb("hid_hi", [P, K, TILES * P], F32R)
        hid_lo = sb("hid_lo", [P, K, TILES * P], F32R)
        pre = sb("pre", [P, 2, D])
        stats = sb("stats", [P, TILES, 6])
        mean_var = sb("mean_var", [P, TILES, 2])
        var_eps = sb("var_eps", [P, TILES])
        newton = sb("newton", [P, TILES])
        inv_std = sb("inv_std", [P, TILES])
        shift = sb("shift", [P, TILES])

        ps_g1 = [ps(f"ps_g1_{i}") for i in range(2)]
        ps_g2 = [ps(f"ps_g2_{i}") for i in range(2)]
        ps_agg = [ps(f"ps_agg_{i}") for i in range(2)]
        ps_T = [ps(f"ps_T_{i}") for i in range(2)]
        behind = [t[:, k, :] for t in (hT_hi, hT_lo, hid_hi, hid_lo) for k in range(K)]
        assert 2 * GC <= len(behind)

        piece = rows[:, 0:2 * PIECE // D, :].rearrange("p a d -> p (a d)").bitcast(I32)
        piece_no = h[:, :, :].rearrange("p a d -> p (a d)")[:, 0:PIECE]
        earlier = extra.gath[:, :, :].rearrange("p a d -> p (a d)")[:, 0:PIECE]

        edges_copied = sem("edges_copied")
        falls_step = sem("falls_step")
        falls_summed = sem("falls_summed")
        order_known = sem("order_known")
        number_loaded = sem("number_loaded")
        piece_loaded = sem("piece_loaded")
        piece_used = sem("piece_used")
        rank_step = sem("rank_step")
        ranked = sem("ranked")
        picked = sem("picked")
        scattered = sem("scattered")
        granules_sorted = sem("granules_sorted")
        const_loaded = sem("const_loaded")
        granules_loaded = sem("granules_loaded")
        w_loaded = sem("w_loaded")
        b_loaded = sem("b_loaded")
        zeroed = sem("zeroed")
        behind_ready = sem("behind_ready")
        behind_summed = sem("behind_summed")
        counted = sem("counted")
        turned = sem("turned")
        turned_read = sem("turned_read")
        rowed = sem("rowed")
        table_ready = sem("table_ready")
        w_hi_ready = sem("w_hi_ready")
        w_ready = sem("w_ready")
        setup_step = sem("setup_step")
        passed = sem("passed")
        x_loaded = sem("x_loaded")
        T_done = sem("T_done")
        hT_hi_ready = sem("hT_hi_ready")
        hT_lo_ready = sem("hT_lo_ready")
        g1_done = sem("g1_done")
        hid_hi_ready = sem("hid_hi_ready")
        hid_lo_ready = sem("hid_lo_ready")
        g2_done = sem("g2_done")
        g2_read = sem("g2_read")
        res_step = sem("res_step")
        norm_step = sem("norm_step")
        norm_ready = sem("norm_ready")
        normed = sem("normed")
        stored = sem("stored")

        def slot(g, j):
            return bass.ds((g % RING) * TILES + j, 1)

        def extra_rounds(eng, g):
            return extras_before(eng, g), extras_before(eng, g + 1)

        def extras_before(eng, g):
            return eng.value_load(extra_row[0:1, bass.ds(g, 1)], min_val=0, max_val=1 << 20)

        def for_groups(eng, body):
            body(0, FULL, FULL, first_group=True)
            body(1, FULL, FULL)
            if full > 3:
                with eng.Fori(2, full - 1) as g:
                    body(g, FULL, FULL)
            body(full - 1, FULL, TAIL if tail_tiles else None)
            if tail_tiles:
                body(full, TAIL, None)

        def wait_alone(eng, semaphore, value):
            eng.wait_ge(semaphore, value)
            eng.sem_inc(passed, 1)

        def if_unsorted(eng):
            eng.wait_ge(order_known, 1)
            return eng.If(eng.value_load(unsorted[0:1, 0:1], min_val=0, max_val=n_sort) > 0)

        block = ctx.enter_context(nc.Block())

        @block.sync
        def _(sp):
            def by_granule(pairs):
                return pairs.rearrange("(a p r) c -> p a (r c)", p=P, r=GRAN)

            sp.dma_start(const[:, :], consts).then_inc(const_loaded, 16)
            sp.dma_start(granules[:, :, :], by_granule(edges[0:n_sort, :])).then_inc(granules_loaded, 16)
            sp.dma_start(following[:, :, :], by_granule(edges[1:n_sort + 1, :])).then_inc(granules_loaded, 16)
            sp.dma_start(by_dst, edges).then_inc(edges_copied, 16)
            sp.dma_start(w_raw[:, 0], W1.rearrange("(k p) n -> p k n", p=P)).then_inc(w_loaded, 16)
            sp.dma_start(w_raw[:, 1], W2.rearrange("(k p) n -> p k n", p=P)).then_inc(w_loaded, 16)
            with nc.allow_non_contiguous_dma(reason="a bias of 512 values, once"):
                sp.dma_start(b1_col[:, :], b1.rearrange("(k p) -> p k", p=P)).then_inc(b_loaded, 16)
            sp.dma_start(b2_all[:, :], b2.partition_broadcast(P)).then_inc(b_loaded, 16)

            with if_unsorted(sp):
                sp.dma_start(number[:, :], edge_no).then_inc(number_loaded, 16)
                sp.dma_start(piece_no, in_piece.partition_broadcast(P)).then_inc(number_loaded, 16)

                def load_piece(q):
                    sp.dma_start(piece, edges[bass.ds(q * PIECE, PIECE), :].rearrange("e c -> (e c)")
                                 .partition_broadcast(P)).then_inc(piece_loaded, 16)

                load_piece(0)
                if n_sort > PIECE:
                    with sp.Fori(1, n_sort // PIECE) as q:
                        sp.wait_ge(piece_used, q)
                        load_piece(q)
                sp.wait_ge(scattered, 16 * GC * GRAN)
                sp.dma_start(granules[:, :, :], by_granule(by_dst[0:n_sort, :])).then_inc(granules_sorted, 16)
                sp.wait_ge(granules_sorted, 16)
            sp.wait_ge(edges_copied, 16)

            def load_x(g, shape, slot_used):
                r, n = shape
                if isinstance(g, int) and g == W_GROUP:
                    sp.wait_ge(w_ready, 1)
                if slot_used or g:
                    sp.wait_ge(x_loaded, 16 * g)
                if slot_used:
                    sp.wait_ge(stored, 16 * (g - RING + 1))
                sp.dma_start(rows[0:r, bass.ds((g % RING) * TILES, n), :],
                             x[bass.ds(g * TILES * P, r * n), :].rearrange("(j p) d -> p j d", p=r)
                             ).then_inc(x_loaded, 16)

            def load_record(w, g, skipped, last_used):
                starts = []
                for j in range(TILES):
                    start = sp.value_load(start_row[0:1, bass.ds(g + P * j, 1)], min_val=0, max_val=last_granule)
                    if skipped is not None:
                        start = (start + skipped * PER_WINDOW).with_bounds(min_val=0, max_val=last_granule)
                    starts.append(start * GRAN)
                if last_used is not None:
                    sp.wait_ge(w.idx_ready, last_used)
                for j in range(TILES):
                    sp.dma_start(w.rec[:, j, :], by_dst[bass.ds(starts[j], P), :]).then_inc(w.rec_loaded, 16)
                sp.dma_start(w.rec_low[:, :], tile_low[bass.ds(g, 1), :].partition_broadcast(P)
                             ).then_inc(w.rec_loaded, 16)

            def load_group(g, shape, slot_used):
                load_x(g, shape, slot_used)
                if isinstance(g, int) and g == 0:
                    sp.wait_ge(table_ready, 1)
                    load_record(first, 0, None, None)
                    sp.wait_ge(table_ready, 2)
                    load_extra(0)
                load_record(first, g + 1, None, g + 1)
                if not (isinstance(g, int) and g == 0):
                    load_extra(g)

            def load_extra(g):
                e0, e1 = extra_rounds(sp, g)
                with sp.If(e1 > e0):
                    with sp.Fori(e0, e1) as e:
                        load_record(extra, g, e - e0 + 1, e + extra.ahead)

            for g in range(min(RING, full)):
                load_group(g, FULL, False)
            if full > RING:
                with sp.Fori(RING, full) as g:
                    load_group(g, FULL, True)
            if tail_tiles:
                load_group(full, TAIL, full >= RING)

        @block.gpsimd
        def _(pool):
            nc.gpsimd.memset(ones[:, :], 1.0).then_inc(zeroed, 1)
            nc.gpsimd.memset(first.gath[:, :, :], 0.0).then_inc(zeroed, 1)
            nc.gpsimd.memset(extra.gath[:, :, :], 0.0).then_inc(zeroed, 1)
            pool.wait_ge(zeroed, 3)
            with if_unsorted(pool):
                pool.wait_ge(edges_copied, 16)
                pool.wait_ge(ranked, 1)
                last_place = pool.to_reg(n_sort - 1)

                for a in range(GC):
                    def column(i, r, first):
                        if not first:
                            pool.wait_ge(scattered, 16 * i)
                        nc.gpsimd.tensor_copy(pair[:, :], granules[:, a, bass.ds(2 * r, 2)]).then_inc(picked, 1)
                        nc.gpsimd.tensor_copy(pair_rank[:, :], rank_i[:, bass.ds(i, 1)]).then_inc(picked, 1)
                        wait_alone(pool, picked, 2 * i + 2)
                        nc.gpsimd.indirect_dma_start(
                            out=by_dst, out_offset=bass.IndirectOffsetOnAxis(ap=pair_rank[:, :], axis=0),
                            in_=pair[:, :], in_offset=None, bounds_check=last_place,
                            oob_is_err=False).then_inc(scattered, 16)

                    column(a * GRAN, 0, first=a == 0)
                    with pool.Fori(1, GRAN) as r:
                        column(r + a * GRAN, r, first=False)
            pool.wait_ge(table_ready, 2)
            last_row = pool.to_reg(N - 1)

            def gather(w, n, again=True):
                pool.wait_ge(w.idx_ready, n + 1 + w.ahead)
                for j in range(TILES):
                    if again:
                        wait_alone(pool, w.lo_ready, w.round_before(n, j))
                    nc.gpsimd.indirect_dma_start(
                        out=w.gath[:, j, :], out_offset=None, in_=x,
                        in_offset=bass.IndirectOffsetOnAxis(ap=w.row_idx[:, j:j + 1], axis=0),
                        bounds_check=last_row, oob_is_err=False).then_inc(w.gathered[j], 16)

            def split_gathered(w, n):
                for j in range(TILES):
                    pool.wait_ge(w.hi_ready, (n + w.ahead) * TILES + j + 1)
                    pool.wait_ge(w.agg_done, w.round_before(n, j))
                    nc.gpsimd.tensor_tensor(w.gath_lo[:, j, :], w.gath[:, j, :],
                                            w.gath_hi[:, j, :].bitcast(F32),
                                            ALU.subtract).then_inc(w.lo_ready, 1)

            def gather_group(g):
                gather(first, g)
                e0, e1 = extra_rounds(pool, g)
                with pool.If(e1 > e0):
                    gather(extra, e0)
                split_gathered(first, g)
                with pool.If(e1 > e0):
                    split_gathered(extra, e0)
                    with pool.If(e1 > e0 + 1):
                        with pool.Fori(e0 + 1, e1) as e:
                            gather(extra, e)

            gather(first, 0, again=False)
            e0, e1 = extra_rounds(pool, 0)
            with pool.If(e1 > e0):
                with pool.Fori(e0, e1) as e:
                    gather(extra, e)
            with pool.Fori(1, groups) as g:
                gather_group(g)

        @block.scalar
        def _(act):
            act.sem_inc(extra.hi_ready, extra.ahead * TILES)
            act.wait_ge(w_loaded, 32)
            nc.scalar.copy(w_hi[:, 0], w_raw[:, 0]).then_inc(w_hi_ready, 1)
            nc.scalar.copy(w_hi[:, 1], w_raw[:, 1]).then_inc(w_hi_ready, 1)
            act.wait_ge(b_loaded, 32)
            act.wait_ge(table_ready, 2)

            def split_gathered(w, n, again=True):
                for j in range(TILES):
                    act.wait_ge(w.gathered[j], (n + 1) * 16)
                    if again:
                        act.wait_ge(w.agg_done, w.round_before(n, j))
                    nc.scalar.copy(w.gath_hi[:, j, :], w.gath[:, j, :]).then_inc(w.hi_ready, 1)

            def first_extra(e0, e1):
                with act.If(e1 > e0):
                    split_gathered(extra, e0)

            def more_extra(e0, e1):
                with act.If(e1 > e0 + 1):
                    with act.Fori(e0 + 1, e1) as e:
                        split_gathered(extra, e)

            def split_hT(g, shape, k):
                c = shape[0] * shape[1]
                act.wait_ge(T_done, g * K + k + 1)
                nc.scalar.copy(hT_hi[:, k, 0:c], ps_T[k % 2][:, 0:c]).then_inc(hT_hi_ready, 1)

            def hidden(g, shape, m):
                c = shape[0] * shape[1]
                act.wait_ge(g1_done, g * K + m + 1)
                act.wait_ge(hid_lo_ready, g * K + (m - 1 if m > 1 else 0))
                nc.scalar.activation(hid[:, m % 2, 0:c], ps_g1[m % 2][:, 0:c], ACT.Relu,
                                     bias=b1_col[:, m:m + 1])
                if m == 0:
                    act.wait_ge(g2_done, g * TILES)
                nc.scalar.activation(hid_hi[:, m, 0:c], ps_g1[m % 2][:, 0:c], ACT.Relu,
                                     bias=b1_col[:, m:m + 1]).then_inc(hid_hi_ready, 1)

            def normalise(g, shape):
                r, n = shape
                act.wait_ge(norm_ready, g + 1)
                for j in range(n):
                    y = rows[0:r, slot(g, j), :]
                    nc.scalar.activation(y, y, ACT.Identity, bias=shift[0:r, j:j + 1],
                                         scale=inv_std[0:r, j:j + 1]).then_inc(normed, 1)

            def store(g, shape):
                r, n = shape
                act.wait_ge(normed, g * TILES + n)
                act.wait_ge(stored, g * 16)
                act.dma_start(out[bass.ds(g * TILES * P, r * n), :].rearrange("(j p) d -> p j d", p=r),
                              rows[0:r, bass.ds((g % RING) * TILES, n), :]).then_inc(stored, 16)

            def body(g, shape, then, first_group=False):
                hidden(g, shape, 0)
                if then:
                    split_gathered(first, g + 1)
                hidden(g, shape, 1)
                if then:
                    e0, e1 = extra_rounds(act, g + 1)
                    first_extra(e0, e1)
                hidden(g, shape, 2)
                hidden(g, shape, 3)
                if then:
                    more_extra(e0, e1)
                if not first_group:
                    normalise(g - 1, FULL)
                    store(g - 1, FULL)
                if then:
                    act.wait_ge(g1_done, g * K + K)
                    for k in range(K):
                        split_hT(g + 1, then, k)

            split_gathered(first, 0, again=False)
            e0, e1 = extra_rounds(act, 0)
            first_extra(e0, e1)
            more_extra(e0, e1)
            for k in range(K):
                split_hT(0, FULL, k)
            for_groups(act, body)
            g, shape = (full, TAIL) if tail_tiles else (full - 1, FULL)
            normalise(g, shape)
            store(g, shape)
            act.wait_ge(stored, 16 * groups)

        @block.vector
        def _(dve):
            steps = [0]

            def step(ins):
                steps[0] += 1
                ins.then_inc(setup_step, 1)
                dve.wait_ge(setup_step, steps[0])

            dve.wait_ge(const_loaded, 16)
            dve.wait_ge(granules_loaded, 32)
            nc.vector.tensor_tensor(falls[:, :, :], following[:, :, 1:2 * GRAN:2], granules[:, :, 1:2 * GRAN:2],
                                    ALU.is_lt).then_inc(falls_step, 1)
            dve.wait_ge(falls_step, 1)
            nc.vector.tensor_reduce(n_falls[:, :], falls[:, :, :], AX.XY, ALU.add).then_inc(falls_step, 1)
            dve.wait_ge(falls_summed, 1)
            nc.vector.tensor_copy(unsorted[:, :], ps_agg[0][0:1, 0:1]).then_inc(order_known, 1)

            with if_unsorted(dve):
                nc.vector.memset(rank[:, :], 0.0).then_inc(rank_step, 1)
                dve.wait_ge(number_loaded, 32)
                dve.wait_ge(zeroed, 3)
                columns = GC * GRAN
                per_piece = 2 * columns + 2

                def compare(q):
                    wait_alone(dve, piece_loaded, 16 * (q + 1))
                    for a in range(GC):
                        with dve.Fori(0, GRAN) as r:
                            step_ = q * per_piece + 2 * (r + a * GRAN) + 1
                            dve.wait_ge(rank_step, step_)
                            c = bass.ds(r + a * GRAN, 1)
                            nc.vector.tensor_scalar(earlier, piece_no, number[:, c], None,
                                                    ALU.is_lt).then_inc(rank_step, 1)
                            dve.wait_ge(rank_step, step_ + 1)
                            nc.vector.scalar_tensor_tensor(
                                earlier, piece[:, 1:2 * PIECE:2], granules[:, a, bass.ds(2 * r + 1, 1)], earlier,
                                ALU.subtract, ALU.is_lt, accum_out=rank_part[:, c]).then_inc(rank_step, 1)
                    dve.wait_ge(rank_step, (q + 1) * per_piece - 1)
                    nc.vector.tensor_tensor(rank[:, :], rank[:, :], rank_part[:, :], ALU.add).then_inc(rank_step, 1)
                    nc.vector.tensor_scalar(number[:, :], number[:, :], float(-PIECE), None,
                                            ALU.add).then_inc(rank_step, 1)
                    dve.wait_ge(rank_step, (q + 1) * per_piece + 1)
                    dve.sem_inc(piece_used, 1)

                with dve.Fori(0, n_sort // PIECE) as q:
                    compare(q)
                nc.vector.tensor_copy(rank_i[:, :], rank[:, :]).then_inc(ranked, 1)
                dve.wait_ge(granules_sorted, 16)
            nc.vector.tensor_copy(ends[:, 0, :], granules[:, :, 1])
            step(nc.vector.tensor_copy(ends[:, 1, :], granules[:, :, 2 * GRAN - 1]))
            dve.wait_ge(zeroed, 3)
            nc.vector.tensor_copy(ones_r[:, :], ones[:, :])
            for a in range(GC):
                for e, (end, bound) in enumerate(((1, low_row), (0, high_row))):
                    nc.vector.tensor_scalar(behind[2 * a + e], bound, ends[:, end, a:a + 1], None,
                                            ALU.is_gt).then_inc(behind_ready, 1)
            dve.wait_ge(behind_summed, 1)
            nc.vector.tensor_copy(start_row[0:1, :], ps_g1[0][0:1, :]).then_inc(table_ready, 1)
            dve.wait_ge(table_ready, 1)
            step(nc.vector.scalar_tensor_tensor(n_gran[:, :], ps_g1[1][0:1, :], float(PER_WINDOW - 1),
                                                start_row[0:1, :], ALU.add, ALU.subtract))
            step(nc.vector.tensor_scalar(n_round[:, :], n_gran[:, :], PER_WINDOW.bit_length() - 1, None,
                                         ALU.arith_shift_right))
            step(nc.vector.tensor_reduce(most_rounds[:, :], n_round[:, :].rearrange("o (j g) -> o g j", j=TILES),
                                         AX.X, ALU.max))
            nc.vector.tensor_scalar(n_extra[:, :], most_rounds[:, :], -1.0, 0.0, ALU.add,
                                    ALU.max).then_inc(counted, 1)
            dve.wait_ge(turned, 1)
            nc.vector.tensor_copy(n_extra_col[:, :], ps_g2[0][:, 0:1]).then_inc(turned_read, 1)
            dve.wait_ge(rowed, 1)
            nc.vector.tensor_copy(extra_row[0:1, :], ps_g2[1][0:1, 0:P]).then_inc(table_ready, 1)

            def indices(w, n):
                dve.wait_ge(w.rec_loaded, (n + 1) * (16 * (TILES + 1)))
                nc.vector.tensor_tensor(w.local[:, :], w.rec[:, :, 1], w.rec_low[:, :],
                                        ALU.subtract).then_inc(w.idx_step, 1)
                dve.wait_ge(w.idx_step, n * 3 + 1)
                nc.vector.scalar_tensor_tensor(w.outside[:, :], w.local[:, :], float(P - 1), w.local[:, :],
                                               ALU.subtract, ALU.mult).then_inc(w.idx_step, 1)
                dve.wait_ge(w.idx_step, n * 3 + 2)
                nc.vector.tensor_scalar(w.far[:, :], w.outside[:, :], 0.0, FAR, ALU.is_gt,
                                        ALU.mult).then_inc(w.idx_step, 1)
                dve.wait_ge(w.idx_step, n * 3 + 3)
                nc.vector.tensor_tensor(w.row_idx[:, :], w.far[:, :], w.rec[:, :, 0],
                                        ALU.add).then_inc(w.idx_ready, 1)

            def onehots(w, n):
                dve.wait_ge(w.agg_done, (n + w.ahead) * TILES)
                for j in range(TILES):
                    last = nc.vector.tensor_scalar(w.onehot[:, j, :], node_no, w.local[:, j:j + 1], None,
                                                   ALU.is_equal)
                last.then_inc(w.onehot_ready, 1)

            def next_indices(g):
                for j in range(TILES):
                    dve.wait_ge(first.gathered[j], (g + 1) * 16)
                dve.wait_ge(first.onehot_ready, g + 1)
                dve.wait_ge(first.idx_ready, g + 1)
                indices(first, g + 1)

            def may_add(g):
                dve.wait_ge(x_loaded, (g + 1) * 16)
                dve.wait_ge(T_done, g * K)

            def add_first(g, shape, j):
                r, n = shape
                dve.wait_ge(first.agg_done, g * TILES + j + 1)
                if j < n:
                    nc.vector.tensor_tensor(h[0:r, j, :], ps_agg[j % 2][0:r, :],
                                            rows[0:r, slot(g, j), :], ALU.add).then_inc(first.added, 1)
                else:
                    dve.sem_inc(first.added, 1)

            def begin_extra(g):
                e0, e1 = extra_rounds(dve, g)
                with dve.If(e1 > e0):
                    indices(extra, e0)
                    onehots(extra, e0)

            def split_gathered(w, upto):
                for j in range(TILES):
                    dve.wait_ge(w.hi_ready, w.round_before(upto, j))
                    nc.vector.tensor_tensor(w.gath_lo[:, j, :], w.gath[:, j, :],
                                            w.gath_hi[:, j, :].bitcast(F32),
                                            ALU.subtract).then_inc(w.lo_ready, 1)

            def add_extra(g, shape, upto, tiles):
                r, n = shape
                dve.wait_ge(first.added, (g + 1) * TILES)
                dve.wait_ge(extra.added, upto * TILES)
                for j in tiles:
                    dve.wait_ge(extra.agg_done, upto * TILES + j + 1)
                    if j < n:
                        nc.vector.tensor_tensor(h[0:r, j, :], ps_agg[j % 2][0:r, :], h[0:r, j, :],
                                                ALU.add).then_inc(extra.added, 1)
                    else:
                        dve.sem_inc(extra.added, 1)

            def first_half_extra(g, shape, e0, e1):
                with dve.If(e1 > e0):
                    add_extra(g, shape, e0 + 1, FRONT)

            def next_extra(e):
                for j in range(TILES):
                    dve.wait_ge(extra.gathered[j], e * 16)
                dve.wait_ge(extra.onehot_ready, e)
                dve.wait_ge(extra.idx_ready, e + extra.ahead)
                indices(extra, e)

            def finish_extra(g, shape, begun, e1):
                with dve.If(e1 > begun + 1):
                    with dve.Fori(begun + 1, e1) as e:
                        next_extra(e)
                        split_gathered(extra, e)
                        add_extra(g, shape, e, FRONT + BACK)
                        onehots(extra, e)
                split_gathered(extra, e1)
                add_extra(g, shape, e1, FRONT + BACK)

            def end_extra(g, shape, e0, e1):
                with dve.If(e1 > e0):
                    add_extra(g, shape, e0 + 1, BACK)
                    with dve.If(e1 > e0 + 1):
                        next_extra(e0 + 1)
                        onehots(extra, e0 + 1)
                        finish_extra(g, shape, e0 + 1, e1)

            def split_hT(g, shape, k):
                c = shape[0] * shape[1]
                dve.wait_ge(hT_hi_ready, g * K + k + 1)
                nc.vector.tensor_tensor(hT_lo[:, k, 0:c], ps_T[k % 2][:, 0:c],
                                        hT_hi[:, k, 0:c].bitcast(F32), ALU.subtract).then_inc(hT_lo_ready, 1)

            def hidden(g, shape, m):
                c = shape[0] * shape[1]
                dve.wait_ge(hid_hi_ready, g * K + m + 1)
                nc.vector.tensor_tensor(hid_lo[:, m, 0:c], hid[:, m % 2, 0:c],
                                        hid_hi[:, m, 0:c].bitcast(F32), ALU.subtract).then_inc(hid_lo_ready, 1)

            def add_bias(g, shape, t):
                r, n = shape
                if t < n:
                    dve.wait_ge(g2_done, g * TILES + t + 1)
                    nc.vector.tensor_tensor(pre[0:r, t % 2, :], ps_g2[t % 2][0:r, :], b2_all[0:r, :],
                                            ALU.add).then_inc(g2_read, 1)

            def residual(g, shape, t):
                r, n = shape
                if t < n:
                    dve.wait_ge(g2_read, g * TILES + t + 1)
                    y = rows[0:r, slot(g, t), :]
                    nc.vector.scalar_tensor_tensor(y, pre[0:r, t % 2:t % 2 + 1, :], 0.0, y, ALU.max,
                                                   ALU.add).then_inc(res_step, 1)

            def statistics(g, shape, t):
                r, n = shape
                if t < n:
                    wait_alone(dve, res_step, (g * TILES + t) * 2 + 1)
                    nc.vector.bn_stats(stats[0:r, t, :], rows[0:r, slot(g, t), :]).then_inc(res_step, 1)

            def mean_and_variance(g, shape, t):
                r, n = shape
                if t < n:
                    if t == 0:
                        dve.wait_ge(norm_ready, g)
                    wait_alone(dve, res_step, (g * TILES + t) * 2 + 2)
                    last = nc.vector.bn_aggr(mean_var[0:r, t, :], stats[0:r, t, :])
                    if t == n - 1:
                        last.then_inc(norm_step, 1)
                        dve.wait_ge(norm_step, g * NORM_STEPS + 1)
                        nc.vector.tensor_scalar(var_eps[0:r, 0:n], mean_var[0:r, 0:n, 1], EPS, None,
                                                ALU.add).then_inc(norm_step, 1)

            def norm_factors(g, shape):
                r, n = shape

                def link(i, ins):
                    ins.then_inc(norm_step, 1)
                    dve.wait_ge(norm_step, g * NORM_STEPS + i)

                y, t, v = inv_std[0:r, 0:n], newton[0:r, 0:n], var_eps[0:r, 0:n]
                dve.wait_ge(norm_step, g * NORM_STEPS + 2)
                dve.wait_ge(normed, g * TILES)
                link(3, nc.vector.tensor_scalar(newton[0:r, 0:n].bitcast(I32), v.bitcast(I32), 1, None,
                                                ALU.arith_shift_right))
                link(4, nc.vector.tensor_scalar(y.bitcast(I32), t.bitcast(I32), -1.0, RSQRT_GUESS,
                                                ALU.mult, ALU.add))
                for i in range(NEWTONS):
                    link(5 + 3 * i, nc.vector.tensor_tensor(t, y, y, ALU.mult))
                    link(6 + 3 * i, nc.vector.scalar_tensor_tensor(t, t, -0.5, v, ALU.mult, ALU.mult))
                    link(7 + 3 * i, nc.vector.scalar_tensor_tensor(y, t, 1.5, y, ALU.add, ALU.mult))
                nc.vector.scalar_tensor_tensor(shift[0:r, 0:n], mean_var[0:r, 0:n, 0], -1.0,
                                               y, ALU.mult, ALU.mult).then_inc(norm_ready, 1)

            def body(g, shape, then, first_group=False):
                if not first_group:
                    norm_factors(g - 1, FULL)
                hidden(g, shape, 0)
                if then:
                    onehots(first, g + 1)
                    next_indices(g + 1)
                hidden(g, shape, 1)
                if then:
                    e0, e1 = extra_rounds(dve, g + 1)
                hidden(g, shape, 2)
                hidden(g, shape, 3)
                if then:
                    may_add(g + 1)
                    add_first(g + 1, then, 0)
                    add_first(g + 1, then, 1)
                add_bias(g, shape, 0)
                if then:
                    add_first(g + 1, then, 2)
                residual(g, shape, 0)
                if then:
                    add_first(g + 1, then, 3)
                statistics(g, shape, 0)
                add_bias(g, shape, 1)
                if then:
                    first_half_extra(g + 1, then, e0, e1)
                mean_and_variance(g, shape, 0)
                residual(g, shape, 1)
                statistics(g, shape, 1)
                add_bias(g, shape, 2)
                if then:
                    end_extra(g + 1, then, e0, e1)
                mean_and_variance(g, shape, 1)
                residual(g, shape, 2)
                if then:
                    split_hT(g + 1, then, 0)
                statistics(g, shape, 2)
                if then:
                    split_hT(g + 1, then, 1)
                    begin_extra(g + 2)
                mean_and_variance(g, shape, 2)
                if then:
                    split_hT(g + 1, then, 2)
                    split_hT(g + 1, then, 3)
                add_bias(g, shape, 3)
                residual(g, shape, 3)
                statistics(g, shape, 3)
                mean_and_variance(g, shape, 3)

            dve.wait_ge(table_ready, 2)
            dve.sem_inc(extra.idx_ready, extra.ahead)
            dve.sem_inc(extra.lo_ready, extra.ahead * TILES)
            dve.sem_inc(extra.added, extra.ahead * TILES)
            indices(first, 0)
            dve.wait_ge(w_hi_ready, 2)
            for i in range(2):
                last = nc.vector.tensor_tensor(w_lo[:, i], w_raw[:, i], w_hi[:, i].bitcast(F32), ALU.subtract)
            last.then_inc(w_ready, 1)
            onehots(first, 0)
            begin_extra(0)
            split_gathered(first, 1)
            may_add(0)
            for j in range(TILES):
                add_first(0, FULL, j)
            e0, e1 = extra_rounds(dve, 0)
            with dve.If(e1 > e0):
                finish_extra(0, FULL, e0, e1)
            next_indices(0)
            begin_extra(1)
            for k in range(K):
                split_hT(0, FULL, k)
            dve.wait_ge(b_loaded, 32)
            for_groups(dve, body)
            norm_factors(*((full, TAIL) if tail_tiles else (full - 1, FULL)))

        @block.tensor
        def _(pe):
            pe.sem_inc(extra.agg_done, extra.ahead * TILES)
            pe.wait_ge(zeroed, 3)
            pe.wait_ge(falls_step, 2)
            nc.tensor.matmul(ps_agg[0][0:1, 0:1], n_falls[:, :], ones[:, 0:1], start=True,
                             stop=True).then_inc(falls_summed, 1)
            for a in range(GC):
                for e in range(2):
                    pe.wait_ge(behind_ready, 2 * a + e + 1)
                    last = nc.tensor.matmul(ps_g1[e][:, :], ones_r[:, :], behind[2 * a + e],
                                            start=a == 0, stop=a == GC - 1)
            last.then_inc(behind_summed, 1)
            pe.wait_ge(counted, 1)
            nc.tensor.matmul(ps_g2[0][:, 0:1], n_extra[0:1, :], ones[0:1, 0:1], start=True,
                             stop=True).then_inc(turned, 1)
            pe.wait_ge(turned_read, 1)
            nc.tensor.matmul(ps_g2[1][0:1, 0:P], n_extra_col[:, :], before, start=True,
                             stop=True).then_inc(rowed, 1)
            pe.wait_ge(table_ready, 2)
            pe.wait_ge(w_ready, 1)

            def product(out_, a_hi, a_lo, b_hi, b_lo, start, stop):
                nc.tensor.matmul(out_, a_hi, b_hi, start=start, stop=False)
                nc.tensor.matmul(out_, a_hi, b_lo, start=False, stop=False)
                return nc.tensor.matmul(out_, a_lo, b_hi, start=False, stop=stop)

            def aggregate(w, upto, shape, tiles):
                r = shape[0]
                pe.wait_ge(w.onehot_ready, upto)
                before_it = (upto if w.ahead else upto - 1) * TILES
                for j in tiles:
                    pe.wait_ge(w.lo_ready, before_it + j + 1)
                    pe.wait_ge(w.added, before_it + (j - 1 if j > 1 else 0))
                    nc.tensor.matmul(ps_agg[j % 2][0:r, :], w.onehot[:, j, 0:r], w.gath_hi[:, j, :],
                                     start=True, stop=False)
                    nc.tensor.matmul(ps_agg[j % 2][0:r, :], w.onehot[:, j, 0:r], w.gath_lo[:, j, :],
                                     start=False, stop=True).then_inc(w.agg_done, 1)

            def first_half_extra(g, shape, e0, e1):
                with pe.If(e1 > e0):
                    pe.wait_ge(first.added, (g + 1) * TILES)
                    aggregate(extra, e0 + 1, shape, FRONT)

            def end_extra(g, shape, e0, e1):
                with pe.If(e1 > e0):
                    with pe.If(e1 > e0 + 1):
                        with pe.Fori(e0 + 1, e1) as e:
                            aggregate(extra, e, shape, BACK)
                            aggregate(extra, e + 1, shape, FRONT)
                    aggregate(extra, e1, shape, BACK)

            def h_is_whole(g, e1):
                pe.wait_ge(first.added, (g + 1) * TILES)
                pe.wait_ge(extra.added, (e1 + extra.ahead) * TILES)

            def transposes(g, shape, k):
                r, n = shape
                pe.wait_ge(hT_lo_ready, g * K + (k - 1 if k > 1 else 0))
                for j in range(n):
                    last = nc.tensor.transpose(ps_T[k % 2][:, j * r:(j + 1) * r],
                                               h[0:r, j, k * P:(k + 1) * P], ident[0:r, 0:r])
                last.then_inc(T_done, 1)

            def first_product(g, shape, m):
                c = shape[0] * shape[1]
                pe.wait_ge(hid_hi_ready, g * K + (m - 1 if m > 1 else 0))
                for k in range(K):
                    if m == 0:
                        pe.wait_ge(hT_lo_ready, g * K + k + 1)
                    last = product(ps_g1[m % 2][:, 0:c],
                                   w_hi[:, 0, k, m * P:(m + 1) * P], w_lo[:, 0, k, m * P:(m + 1) * P],
                                   hT_hi[:, k, 0:c], hT_lo[:, k, 0:c], k == 0, k == K - 1)
                last.then_inc(g1_done, 1)

            def second_product(g, shape, t):
                r, n = shape
                if t >= n:
                    return
                pe.wait_ge(g2_read, g * TILES + (t - 1 if t > 1 else 0))
                for k in range(K):
                    if t == 0:
                        pe.wait_ge(hid_lo_ready, g * K + k + 1)
                    last = product(ps_g2[t % 2][0:r, :],
                                   hid_hi[:, k, t * r:(t + 1) * r], hid_lo[:, k, t * r:(t + 1) * r],
                                   w_hi[:, 1, k, :], w_lo[:, 1, k, :], k == 0, k == K - 1)
                last.then_inc(g2_done, 1)

            def body(g, shape, then, first_group=False):
                for m in range(K):
                    first_product(g, shape, m)
                if then:
                    e0, e1 = extra_rounds(pe, g + 1)
                    aggregate(first, g + 2, then, FRONT)
                second_product(g, shape, 0)
                if then:
                    aggregate(first, g + 2, then, BACK)
                second_product(g, shape, 1)
                if then:
                    first_half_extra(g + 1, then, e0, e1)
                second_product(g, shape, 2)
                if then:
                    end_extra(g + 1, then, e0, e1)
                    h_is_whole(g + 1, e1)
                    transposes(g + 1, then, 0)
                    transposes(g + 1, then, 1)
                second_product(g, shape, 3)
                if then:
                    transposes(g + 1, then, 2)
                    transposes(g + 1, then, 3)

            aggregate(first, 1, FULL, FRONT + BACK)
            e0, e1 = extra_rounds(pe, 0)
            first_half_extra(0, FULL, e0, e1)
            end_extra(0, FULL, e0, e1)
            h_is_whole(0, e1)
            for k in range(K):
                transposes(0, FULL, k)
            for_groups(pe, body)


def kernel(x, src, dst, L0_gnn_W1, L0_gnn_b1, L0_gnn_W2, L0_gnn_b2):
    import concourse.bacc as bacc
    from concourse.bass_utils import run_bass_kernel_spmd

    x = np.ascontiguousarray(x)
    n_nodes, n_edges = x.shape[0], src.shape[0]
    full, tail_rows, tail_tiles = plan(n_nodes)
    GC = -(-(-(-n_edges // GRAN) + PER_WINDOW) // P)
    edges = np.full((2 * GC * P * GRAN, 2), int(NO_NODE), np.int32)
    edges[:n_edges, 0], edges[:n_edges, 1] = src, dst
    low = np.full((P, TILES), float(n_nodes), np.float32)
    high = low.copy()
    for g in range(full):
        low[g] = (g * TILES + np.arange(TILES)) * P
        high[g] = low[g] + P
    for j in range(tail_tiles):
        low[full, j] = full * TILES * P + j * tail_rows
        high[full, j] = low[full, j] + tail_rows
    i = np.arange(P)
    consts = np.concatenate([np.eye(P), i[:, None] < i[None, :], np.tile(i, (P, 1)),
                             np.tile(low.T.reshape(-1), (P, 1)), np.tile(high.T.reshape(-1), (P, 1))],
                            axis=1).astype(np.float32)
    edge_no = np.arange(GC * P * GRAN, dtype=np.float32).reshape(GC, P, GRAN).transpose(1, 0, 2).reshape(P, -1)
    arrays = {"x": x, "edges": edges, "W1": L0_gnn_W1, "b1": L0_gnn_b1, "W2": L0_gnn_W2, "b2": L0_gnn_b2,
              "tile_low": low, "consts": consts, "edge_no": edge_no, "in_piece": np.arange(PIECE, dtype=np.float32)}
    arrays = {k: np.ascontiguousarray(v) for k, v in arrays.items()}
    nc = bacc.Bacc("TRN2", target_bir_lowering=False, num_devices=1)
    args = [nc.dram_tensor(f"in_{k}", a.shape, mybir.dt.from_np(a.dtype), kind="ExternalInput").ap()
            for k, a in arrays.items()]
    out = nc.dram_tensor("out_0", x.shape, F32, kind="ExternalOutput").ap()
    gnn_layer(nc, *args, out)
    r = run_bass_kernel_spmd(nc, [{f"in_{k}": a for k, a in arrays.items()}], core_ids=[0])
    return r.results[0]["out_0"]
```
